# Optimizing a Trainium2 kernel written in Bass

```python
import numpy as np
import jax
import jax.numpy as jnp

def _softmax(x, axis=-1):
    return jax.nn.softmax(x, axis=axis)

def _gelu(x):
    return jax.nn.gelu(x, approximate=True)

def _silu(x):
    return jax.nn.silu(x)

def _sigmoid(x):
    return jax.nn.sigmoid(x)

def _layernorm(x, axis=-1, eps=1e-05):
    m = jnp.mean(x, axis=axis, keepdims=True)
    v = jnp.var(x, axis=axis, keepdims=True)
    return (x - m) / jnp.sqrt(v + eps)

def _scatter_add(tgt, idx, src, axis=0):
    return tgt.at[idx].add(src)

def _segment_sum(src, seg, n):
    return jax.ops.segment_sum(src, seg, n)
kernel_name = 'mk_gnn_ffn_d1_gnn_r16_c94e8f'

def setup_inputs(seed: int=0):
    np.random.seed(seed)
    _w = jnp.asarray

    def _rec_inputs():
        import jax
        import jax.numpy as jnp
        _gk = jax.random.key(seed)
        x = -0.000364 + 1 * jax.random.normal(jax.random.fold_in(_gk, 1), (3125, 768), jnp.float32)
        src = jax.random.randint(jax.random.fold_in(_gk, 2), (50000,), 0, 3125, jnp.int32)
        dst = jax.random.randint(jax.random.fold_in(_gk, 3), (50000,), 0, 3125, jnp.int32)
        _o = jnp.argsort(dst, stable=True)
        src = src[_o]
        dst = dst[_o]
        return (x, src, dst)
    x, src, dst = _rec_inputs()

    def _L0_gnn_setup():
        import jax, jax.numpy as jnp
        import numpy as np
        N = 1250
        E_RAND = 20000
        NEG_SLOPE = 0.2

        def gat_layer(x, W, a_src, a_dst, bias, src, dst, heads, out_c, concat):
            n = x.shape[0]
            h = (x @ W).reshape(n, heads, out_c)
            al_s = jnp.einsum('nhc,hc->nh', h, a_src)
            al_d = jnp.einsum('nhc,hc->nh', h, a_dst)
            e = jax.nn.leaky_relu(al_s[src] + al_d[dst], NEG_SLOPE)
            m = jax.ops.segment_max(e, dst, num_segments=n)
            ex = jnp.exp(e - m[dst])
            z = jax.ops.segment_sum(ex, dst, num_segments=n)
            alpha = ex / (z[dst] + 1e-16)
            msg = h[src] * alpha[:, :, None]
            out = jax.ops.segment_sum(msg, dst, num_segments=n)
            out = out.reshape(n, heads * out_c) if concat else out.mean(axis=1)
            return out + bias
        key = jax.random.key(seed)
        ks = jax.random.split(key, 10)
        x = jax.random.normal(ks[0], (N, 768), dtype=jnp.float32)
        src = jax.random.randint(ks[1], (E_RAND,), 0, N)
        dst = jax.random.randint(ks[2], (E_RAND,), 0, N)
        loop = jnp.arange(N)
        edge_index = jnp.stack([jnp.concatenate([src, loop]), jnp.concatenate([dst, loop])])
        s = 1.0 / np.sqrt(768.0)
        W1 = jax.random.normal(ks[3], (768, 768), dtype=jnp.float32) * s
        a_src1 = jax.random.normal(ks[4], (8, 96), dtype=jnp.float32) * 0.1
        a_dst1 = jax.random.normal(ks[5], (8, 96), dtype=jnp.float32) * 0.1
        b1 = jnp.zeros((768,), dtype=jnp.float32)
        W2 = jax.random.normal(ks[6], (768, 768), dtype=jnp.float32) * s
        a_src2 = jax.random.normal(ks[7], (1, 768), dtype=jnp.float32) * 0.1
        a_dst2 = jax.random.normal(ks[8], (1, 768), dtype=jnp.float32) * 0.1
        b2 = jnp.zeros((768,), dtype=jnp.float32)
        return {'x': x, 'edge_index': edge_index, 'W1': W1, 'a_src1': a_src1, 'a_dst1': a_dst1, 'b1': b1, 'W2': W2, 'a_src2': a_src2, 'a_dst2': a_dst2, 'b2': b2}
    _L0_gnn_all = _L0_gnn_setup()
    _L0_gnn_in = {k: v for k, v in _L0_gnn_all.items() if k in ('W1', 'a_src1', 'a_dst1', 'b1', 'W2', 'a_src2', 'a_dst2', 'b2')}
    del _L0_gnn_all

    def _L0_ffn_setup():
        import jax, jax.numpy as jnp
        import numpy as np
        B, T, C, H, E, TOPK, DR = (2, 128, 768, 192, 8, 2, 24)

        def _normalize(v, axis=-1, eps=1e-12):
            return v / jnp.maximum(jnp.linalg.norm(v, axis=axis, keepdims=True), eps)
        key = jax.random.key(seed)
        ks = jax.random.split(key, 16)
        std = 0.02
        n = lambda k, shape, s=std: (s * jax.random.normal(k, shape)).astype(jnp.float32)
        emb = jax.random.normal(ks[3], (E, DR), dtype=jnp.float32)
        emb = emb / (jnp.linalg.norm(emb, axis=-1, keepdims=True) + 1e-08)
        return {'x': jax.random.normal(ks[0], (B, T, C), dtype=jnp.float32), 'router_w': n(ks[1], (E, C)), 'probe_w': n(ks[2], (DR, C)), 'router_emb': emb, 'fatigue': jnp.zeros((E,), jnp.float32), 'energy': jnp.ones((E,), jnp.float32), 'w_fast1': n(ks[4], (E, C, H)), 'w_slow1': n(ks[5], (E, C, H)), 'h_fast1': n(ks[6], (E, C, H), 0.005), 'm_gate1': jax.random.uniform(ks[7], (E,), dtype=jnp.float32), 'b1': jnp.zeros((E, H), jnp.float32), 'w_fast2': n(ks[8], (E, H, C)), 'w_slow2': n(ks[9], (E, H, C)), 'h_fast2': n(ks[10], (E, H, C), 0.005), 'm_gate2': jax.random.uniform(ks[11], (E,), dtype=jnp.float32), 'b2': jnp.zeros((E, C), jnp.float32)}
    _L0_ffn_all = _L0_ffn_setup()
    _L0_ffn_in = {k: v for k, v in _L0_ffn_all.items() if k in ('router_w', 'probe_w', 'router_emb', 'fatigue', 'energy', 'w_fast1', 'w_slow1', 'h_fast1', 'm_gate1', 'b1', 'w_fast2', 'w_slow2', 'h_fast2', 'm_gate2', 'b2')}
    del _L0_ffn_all
    return {'x': x, 'src': src, 'dst': dst, 'L0_gnn_W1': _L0_gnn_in['W1'], 'L0_gnn_a_src1': _L0_gnn_in['a_src1'], 'L0_gnn_a_dst1': _L0_gnn_in['a_dst1'], 'L0_gnn_b1': _L0_gnn_in['b1'], 'L0_gnn_W2': _L0_gnn_in['W2'], 'L0_gnn_a_src2': _L0_gnn_in['a_src2'], 'L0_gnn_a_dst2': _L0_gnn_in['a_dst2'], 'L0_gnn_b2': _L0_gnn_in['b2'], 'L0_ffn_router_w': _L0_ffn_in['router_w'], 'L0_ffn_probe_w': _L0_ffn_in['probe_w'], 'L0_ffn_router_emb': _L0_ffn_in['router_emb'], 'L0_ffn_fatigue': _L0_ffn_in['fatigue'], 'L0_ffn_energy': _L0_ffn_in['energy'], 'L0_ffn_w_fast1': _L0_ffn_in['w_fast1'], 'L0_ffn_w_slow1': _L0_ffn_in['w_slow1'], 'L0_ffn_h_fast1': _L0_ffn_in['h_fast1'], 'L0_ffn_m_gate1': _L0_ffn_in['m_gate1'], 'L0_ffn_b1': _L0_ffn_in['b1'], 'L0_ffn_w_fast2': _L0_ffn_in['w_fast2'], 'L0_ffn_w_slow2': _L0_ffn_in['w_slow2'], 'L0_ffn_h_fast2': _L0_ffn_in['h_fast2'], 'L0_ffn_m_gate2': _L0_ffn_in['m_gate2'], 'L0_ffn_b2': _L0_ffn_in['b2']}

def reference(x, src, dst, L0_gnn_W1, L0_gnn_a_src1, L0_gnn_a_dst1, L0_gnn_b1, L0_gnn_W2, L0_gnn_a_src2, L0_gnn_a_dst2, L0_gnn_b2, L0_ffn_router_w, L0_ffn_probe_w, L0_ffn_router_emb, L0_ffn_fatigue, L0_ffn_energy, L0_ffn_w_fast1, L0_ffn_w_slow1, L0_ffn_h_fast1, L0_ffn_m_gate1, L0_ffn_b1, L0_ffn_w_fast2, L0_ffn_w_slow2, L0_ffn_h_fast2, L0_ffn_m_gate2, L0_ffn_b2):
    import jax
    import jax.numpy as jnp

    def _L0_gnn_ref(x, edge_index, W1, a_src1, a_dst1, b1, W2, a_src2, a_dst2, b2):
        import jax, jax.numpy as jnp
        import numpy as np
        N = 1250
        E_RAND = 20000
        NEG_SLOPE = 0.2

        def gat_layer(x, W, a_src, a_dst, bias, src, dst, heads, out_c, concat):
            n = x.shape[0]
            h = (x @ W).reshape(n, heads, out_c)
            al_s = jnp.einsum('nhc,hc->nh', h, a_src)
            al_d = jnp.einsum('nhc,hc->nh', h, a_dst)
            e = jax.nn.leaky_relu(al_s[src] + al_d[dst], NEG_SLOPE)
            m = jax.ops.segment_max(e, dst, num_segments=n)
            ex = jnp.exp(e - m[dst])
            z = jax.ops.segment_sum(ex, dst, num_segments=n)
            alpha = ex / (z[dst] + 1e-16)
            msg = h[src] * alpha[:, :, None]
            out = jax.ops.segment_sum(msg, dst, num_segments=n)
            out = out.reshape(n, heads * out_c) if concat else out.mean(axis=1)
            return out + bias
        src, dst = (edge_index[0], edge_index[1])
        h = gat_layer(x, W1, a_src1, a_dst1, b1, src, dst, heads=8, out_c=96, concat=True)
        h = jax.nn.elu(h)
        out = gat_layer(h, W2, a_src2, a_dst2, b2, src, dst, heads=1, out_c=768, concat=False)
        return out

    def _L0_ffn_ref(x, router_w, probe_w, router_emb, fatigue, energy, w_fast1, w_slow1, h_fast1, m_gate1, b1, w_fast2, w_slow2, h_fast2, m_gate2, b2):
        import jax, jax.numpy as jnp
        import numpy as np
        B, T, C, H, E, TOPK, DR = (2, 128, 768, 192, 8, 2, 24)

        def _normalize(v, axis=-1, eps=1e-12):
            return v / jnp.maximum(jnp.linalg.norm(v, axis=axis, keepdims=True), eps)
        Bd, Td, Cd = x.shape
        logits = jnp.einsum('btc,ec->bte', x, router_w)
        tok_proxy = x.mean(axis=-1, keepdims=True)
        router_gain = jnp.linalg.norm(router_emb, axis=-1)
        base_bias = 0.02 * tok_proxy
        gain_bias = 0.02 * tok_proxy * router_gain
        tok_unit = _normalize(jnp.einsum('btc,dc->btd', x, probe_w))
        align_bias = 0.02 * jnp.einsum('btd,ed->bte', tok_unit, _normalize(router_emb))
        logits = logits + base_bias + gain_bias + align_bias + 0.1 * energy - 0.1 * fatigue
        g, idx = jax.lax.top_k(logits, TOPK)
        gates = jax.nn.softmax(g, axis=-1)
        N = Bd * Td
        gates_full = jnp.zeros((N, E), x.dtype).at[jnp.arange(N)[:, None], idx.reshape(N, TOPK)].set(gates.reshape(N, TOPK))
        flat_x = x.reshape(N, Cd)

        def body(acc, p):
            wf1, ws1, hf1, mg1, bb1, wf2, ws2, hf2, mg2, bb2, ge = p
            W1 = wf1 + mg1 * ws1 + hf1
            h = jnp.square(jnp.maximum(flat_x @ W1 + bb1, 0.0))
            W2 = wf2 + mg2 * ws2 + hf2
            y = h @ W2 + bb2
            return (acc + ge[:, None] * y, None)
        out, _ = jax.lax.scan(body, jnp.zeros((N, Cd), x.dtype), (w_fast1, w_slow1, h_fast1, m_gate1, b1, w_fast2, w_slow2, h_fast2, m_gate2, b2, gates_full.T))
        return out.reshape(Bd, Td, Cd)
    edge_index = jnp.stack([src, dst])
    x = x + _L0_gnn_ref(_layernorm(x, axis=-1), edge_index, L0_gnn_W1, L0_gnn_a_src1, L0_gnn_a_dst1, L0_gnn_b1, L0_gnn_W2, L0_gnn_a_src2, L0_gnn_a_dst2, L0_gnn_b2)
    x = x + _L0_ffn_ref(_layernorm(x, axis=-1)[None], L0_ffn_router_w, L0_ffn_probe_w, L0_ffn_router_emb, L0_ffn_fatigue, L0_ffn_energy, L0_ffn_w_fast1, L0_ffn_w_slow1, L0_ffn_h_fast1, L0_ffn_m_gate1, L0_ffn_b1, L0_ffn_w_fast2, L0_ffn_w_slow2, L0_ffn_h_fast2, L0_ffn_m_gate2, L0_ffn_b2)[0]
    return x

_drawn_inputs = setup_inputs


def setup_inputs(seed=0):
    import zlib

    import numpy as np

    out = dict(_drawn_inputs(seed))
    spreads = {'L0_gnn_b1': (0.0, 0.1),
     'L0_gnn_b2': (0.0, 0.1),
     'L0_ffn_fatigue': (0.0, 0.49),
     'L0_ffn_energy': (1.0, 0.555),
     'L0_ffn_b1': (0.0, 0.382),
     'L0_ffn_b2': (0.0, 0.1)}
    factors = {'L0_gnn_a_dst2': 2.677, 'L0_ffn_probe_w': 6.951, 'L0_ffn_router_emb': 7.343}
    for name, (base, spread) in spreads.items():
        noise = np.random.default_rng([zlib.crc32(name.encode()), seed]).standard_normal(out[name].shape)
        drawn = base * np.exp(spread * noise) if base else spread * noise
        out[name] = jnp.asarray(drawn.astype(out[name].dtype))
    for name, factor in factors.items():
        out[name] = (out[name] * factor).astype(out[name].dtype)
    return out
```

```python
import concourse.bass as bass
from concourse import mybir
from contextlib import ExitStack

P = 128
N, C, E = 3125, 768, 50000
NB = -(-N // P)
NP = NB * P
KC = C // P
NT = 392
EP = NT * P
RING = 7
UN = 2 * RING
TURNS = NT // UN
HEADS = (8, 1)
ROW = 776
HALF = ROW // 2
NE, HID, DR = 8, 192, 24
EH = NE * HID
HK = EH // P
UNITS = EH * KC // C + HK
SB = 5
SUP = SB * P
NS = NB // SB
SH = SUP // 2
RW = NE + DR + NE + 1
NEG = -1e30
SLOPE = 0.2
LN_EPS = 1e-5
f32, i32, u32, bf16 = mybir.dt.float32, mybir.dt.int32, mybir.dt.uint32, mybir.dt.bfloat16
ALU = mybir.AluOpType
ACT = mybir.ActivationFunctionType
AX = mybir.AxisListType.X
ds = bass.ds


class Steps:

    def __init__(self, eng, sem):
        self.eng, self.sem, self.base, self.n = eng, sem, 0, 0

    def step(self, ins, hold=None):
        self.n += 1
        ins.then_inc(self.sem, 1)
        self.eng.wait_ge(self.sem, self.base + self.n)
        if hold:
            self.eng.sem_inc(hold, 1)

    def loop(self, turn, n):
        self.start, self.size = self.base + self.n, n
        self.base, self.n = turn * n + self.start, 0

    def done(self, turns):
        assert self.n == self.size, (self.n, self.size)
        self.base, self.n = self.start + turns * self.size, 0


def gnn_ffn(nc, io, out, upto=99, dbg=None):
    with ExitStack() as ctx:
        def sb(name, shape, dt=f32):
            return ctx.enter_context(nc.sbuf_tensor(name, shape, dt))

        part_sems, parts_run = [], [0]
        ids = sorted(nc.free_semaphores)

        def sem(name):
            half = len(ids) // 2
            assert len(part_sems) < half
            part_sems.append(nc.alloc_semaphore(name=name, num=ids[parts_run[0] % 2 * half + len(part_sems)]))
            return part_sems[-1]

        def run(part, *args):
            part(*args)
            nc.clear_and_free_semaphores(part_sems)
            part_sems.clear()
            parts_run[0] += 1

        def dram(name, shape):
            if dbg and name in dbg:
                return dbg[name]
            return nc.dram_tensor(name, shape, f32).ap()

        score_tab = [dram(f"score_tab{l}", (NP, HEADS[l])) for l in range(2)]
        first_val = [dram(f"first_val{l}", (EP, HEADS[l])) for l in range(2)]
        edge_ex = [dram(f"edge_ex{l}", (EP, HEADS[l])) for l in range(2)]
        feat_tab = [dram(f"feat_tab{l}", (NP, ROW)) for l in range(2)]
        agg_raw = [dram(f"agg_raw{l}", (NP, ROW)) for l in range(2)]
        mid_rows = dram("mid_rows", (NP, C))
        mid_featT = dram("mid_featT", (NB, P, C))

        big = sb("big", [P, KC * NP])
        featT = big[:, :].rearrange("p (k n) -> p k n", k=KC)
        w1e = big[:, 0:KC * EH].rearrange("p (k n) -> p k n", k=KC)
        w2e = big[:, KC * EH:KC * EH + HK * C].rearrange("p (k n) -> p k n", k=HK)
        wg = sb("wg", [P, KC, C])
        ring = sb("ring", [P, RING * ROW])
        edges = sb("edges", [P, 4 * NT * 8])
        work = sb("work", [P, 2 * ROW + 6 * C])
        at = [0]

        def part(n, of=work):
            at[0] += n
            assert at[0] <= of.shape[1]
            return of[:, at[0] - n:at[0]]

        raw = [part(ROW) for _ in range(2)]
        xn = [part(C) for _ in range(2)]
        tmp = [part(C) for _ in range(2)]
        xT = [part(C).rearrange("p (k n) -> p k n", k=KC) for _ in range(2)]
        onehot = work[:, 2 * ROW:2 * ROW + RING * P].rearrange("p (a n) -> p a n", a=RING)
        onehot_x = work[:, 2 * ROW + RING * P:2 * ROW + (RING + 1) * P]
        zeros = tmp[1][:, 0:HALF]
        sg = tmp[0][:, 0:2 * RING * 8].rearrange("p (a n) -> p a n", a=2)
        iota_f = sb("iota_f", [P, P])
        ident = sb("ident", [P, P])
        blk_base = sb("blk_base", [P, NB])
        src_p = sb("src_p", [P, NT], i32)
        src_t = sb("src_t", [P, NT], i32)
        dst_t = sb("dst_t", [P, NT])
        dst_rel = sb("dst_rel", [P, NT])
        keep = sb("keep", [P, NT])
        rst_f = sb("rst_f", [P, NT])
        rst_b = sb("rst_b", [P, NT])
        bend = sb("bend", [1, NT + 1], i32)
        islot = sb("islot", [P, 2, RING], i32)
        first_idx = sb("first_idx", [P, NB], i32)
        al_node = sb("al_node", [P, NB, 16])
        wa = sb("wa", [P, KC, 16])
        mv = sb("mv", [P, NB, 2])
        rstd = sb("rstd", [P, NB])
        stats = sb("stats", [P, 12])
        carry = sb("carry", [P, 3, 8])
        has = sb("has", [P, 3, 8])
        row_rst = sb("row_rst", [8, 3, P])
        row_scan = sb("row_scan", [8, 3, P + 1])
        small = sb("small", [P, 5, NB])

        acc = ctx.enter_context(nc.psum_tensor("acc", [P, 4, 512], f32))
        tps = ctx.enter_context(nc.psum_tensor("tps", [P, 2, 512], f32))
        mps = ctx.enter_context(nc.psum_tensor("mps", [P, 2, 512], f32))

        def blocks(eng, body, st=None, steps=0, first=0, last=NB):
            n = (last - first) // 2
            with eng.Fori(0, n) as i:
                if st:
                    st.loop(i, 2 * steps)
                body(i * 2 + first, first % 2, i + first // 2)
                body(i * 2 + (first + 1), (first + 1) % 2, i + (first + 1) // 2)
            if st:
                st.done(n)
            if (last - first) % 2:
                body(last - 1, (last - 1) % 2, (last - 1) // 2)

        def load_weights(sp, l, w_in):
            sp.dma_start(wg[:, :, :], io[f"W{l}"].rearrange("(k p) n -> p k n", p=P)).then_inc(w_in, 16)
            sp.dma_start(edges[:, 0:C], io[f"a_src{l}"].partition_broadcast(P)).then_inc(w_in, 16)
            sp.dma_start(edges[:, C:2 * C], io[f"a_dst{l}"].partition_broadcast(P)).then_inc(w_in, 16)

        def attention_weights(dve, st, l, w_in):
            H = HEADS[l]
            dve.wait_ge(w_in, 48)
            for k in range(KC):
                for j in range(2):
                    prod = edges[:, 2 * C + j * C:3 * C + j * C]
                    st.step(nc.vector.tensor_tensor(prod, wg[:, k, :], edges[:, j * C:(j + 1) * C], ALU.mult))
                    st.step(nc.vector.tensor_reduce(wa[:, k, j * H:(j + 1) * H], prod.rearrange("p (h c) -> p h c", h=H),
                                                    AX, ALU.add))

        def setup():
            w_in, x_in, stats_done = sem("w_in0"), [sem("x_in0"), sem("x_in1")], sem("stats_done")
            misc, sqrt_in, sqrt_out = sem("setup_in"), sem("sqrt_in"), sem("sqrt_out")
            chain_v, chain_p, tick_v = sem("setup_dve"), sem("setup_pool"), sem("setup_tick")
            with nc.Block() as block:
                @block.sync
                def _(sp):
                    load_weights(sp, 0, w_in)
                    for dst, name in ((src_p, "src_p"), (src_t, "src_t"), (bend, "bend")):
                        sp.dma_start(dst[:, :], io[name]).then_inc(misc, 16)
                    for sl in range(2):
                        sp.dma_start(raw[sl][:, 0:C], io["x"][sl * P:(sl + 1) * P, :]).then_inc(x_in[sl], 16)

                    def body(b, sl, n):
                        sp.wait_ge(stats_done, b - 1)
                        sp.dma_start(raw[sl][:, 0:C], io["x"][ds(b * P, P), :]).then_inc(x_in[sl], 16)
                    blocks(sp, body, first=2)
                    sp.wait_ge(misc, 48)

                @block.gpsimd
                def _(pool):
                    st = Steps(pool, chain_p)
                    nc.gpsimd.iota(iota_f[:, :], pattern=[[1, P]], base=0, channel_multiplier=0,
                                   allow_small_or_imprecise_dtypes=True)
                    nc.gpsimd.iota(blk_base[:, :], pattern=[[-P, NB]], base=0, channel_multiplier=0,
                                   allow_small_or_imprecise_dtypes=True)
                    st.step(nc.gpsimd.memset(ident[:, :], 0.0))
                    nc.gpsimd.affine_select(out=ident[:, :], in_=ident[:, :], compare_op=ALU.not_equal, fill=1.0,
                                            base=0, pattern=[[-1, P]], channel_multiplier=1)

                @block.scalar
                def _(act):
                    act.wait_ge(sqrt_in, 1)
                    nc.scalar.activation(rstd[:, :], rstd[:, :], ACT.Sqrt).then_inc(sqrt_out, 1)

                @block.vector
                def _(dve):
                    st = Steps(dve, chain_v)

                    def body(b, sl, n):
                        dve.wait_ge(x_in[sl], n * 16 + 16)
                        nc.vector.bn_stats(stats[:, 0:6], raw[sl][:, 0:C // 2])
                        st.step(nc.vector.bn_stats(stats[:, 6:12], raw[sl][:, C // 2:C]), tick_v)
                        st.step(nc.vector.bn_aggr(small[:, 0, 0:2], stats[:, :]))
                        dve.sem_inc(stats_done, 1)
                        st.step(nc.vector.tensor_copy(mv[:, ds(b, 1), :].rearrange("p a b -> p (a b)"), small[:, 0, 0:2]))
                    blocks(dve, body, st, 3)
                    nc.vector.tensor_scalar_add(rstd[:, :], mv[:, :, 1], LN_EPS).then_inc(sqrt_in, 1)
                    attention_weights(dve, st, 0, w_in)
                    dve.wait_ge(sqrt_out, 1)
                    nc.vector.reciprocal(rstd[:, :], rstd[:, :])

        def features(l):
            H = HEADS[l]
            L = f"_f{l}"
            in_ld, row_used = [sem(f"in{j}" + L) for j in range(2)], sem("row_used" + L)
            xn_ready, xT_ps, xT_ready, copied = sem("xn_ready" + L), sem("xT_ps" + L), sem("xT_ready" + L), sem("copied" + L)
            al_ps, al_ready, tab_st, b_in = sem("al_ps" + L), sem("al_ready" + L), sem("tab_st" + L), sem("b_in" + L)
            chain_v, tick_a, tick_p = sem("dve" + L), sem("tick_a" + L), sem("tick_p" + L)
            min_ready, exp_ready, w_in = sem("min" + L), sem("exp" + L), sem("w_in" + L)
            if l == 0:
                row_used = xn_ready
            source, width = (io["x"], C) if l == 0 else (agg_raw[0], ROW)
            bias = edges[:, 3 * NT * 8:3 * NT * 8 + C]
            with nc.Block() as block:
                @block.sync
                def _(sp):
                    if l == 1:
                        load_weights(sp, 1, w_in)
                        sp.dma_start(bias, io["b1g"].partition_broadcast(P)).then_inc(b_in, 16)
                    for sl in range(2):
                        sp.dma_start(raw[sl][:, 0:width], source[sl * P:(sl + 1) * P, :]).then_inc(in_ld[sl], 16)

                    def body(b, sl, n):
                        sp.wait_ge(row_used, b - 1)
                        sp.dma_start(raw[sl][:, 0:width], source[ds(b * P, P), :]).then_inc(in_ld[sl], 16)
                    blocks(sp, body, first=2)
                    sp.wait_ge(al_ready, NB + 1)
                    sp.dma_start(score_tab[l].rearrange("(b p) h -> p b h", p=P), al_node[:, :, 0:H],
                                 allow_slow_non_contiguous=(H == 1)).then_inc(tab_st, 16)
                    sp.wait_ge(tab_st, 16)

                @block.vector
                def _(dve):
                    st = Steps(dve, chain_v)
                    if l == 0:
                        def body(b, sl, n):
                            dve.wait_ge(in_ld[sl], n * 16 + 16)
                            dve.wait_ge(xT_ps, b + 1)
                            nc.vector.tensor_scalar(xn[sl], raw[sl][:, 0:C], mv[:, ds(b, 1), 0], rstd[:, ds(b, 1)],
                                                    ALU.subtract, ALU.mult).then_inc(xn_ready, 1)
                        blocks(dve, body)
                    else:
                        attention_weights(dve, st, 1, w_in)
                        dve.wait_ge(b_in, 16)

                        def first_half(b, sl, n):
                            H0 = HEADS[0]
                            r3 = raw[sl].rearrange("p (h c) -> p h c", h=H0)
                            z, y = r3[:, :, C // H0], tmp[sl].rearrange("p (h c) -> p h c", h=H0)
                            dve.wait_ge(in_ld[sl], n * 16 + 16)
                            st.step(nc.vector.tensor_scalar_add(z, z, 1e-16))
                            st.step(nc.vector.reciprocal(z, z))
                            st.step(nc.vector.tensor_tensor(y, r3[:, :, 0:C // H0],
                                                            z.unsqueeze(2).to_broadcast([P, H0, C // H0]), ALU.mult))
                            dve.sem_inc(row_used, 1)
                            st.step(nc.vector.tensor_tensor(tmp[sl], tmp[sl], bias, ALU.add))
                            dve.wait_ge(xT_ps, b + 1)
                            nc.vector.tensor_scalar_min(xn[sl], tmp[sl], 0.0).then_inc(min_ready, 1)

                        def second_half(b, sl, n):
                            st.step(nc.vector.tensor_scalar(tmp[sl], tmp[sl], 0.0, -1.0, ALU.max, ALU.add))
                            dve.wait_ge(exp_ready, b + 1)
                            nc.vector.tensor_tensor(xn[sl], xn[sl], tmp[sl], ALU.add).then_inc(xn_ready, 1)

                        first_half(0, 0, 0)

                        def body(b, sl, n):
                            first_half(b, sl, n)
                            second_half(b - 1, 1 - sl, None)
                        blocks(dve, body, st, 5, first=1)
                        second_half(NB - 1, (NB - 1) % 2, None)

                @block.tensor
                def _(pe):
                    pe.sem_inc(xT_ps, 2)

                    def body(b, sl, n):
                        pe.wait_ge(xn_ready, b + 1)
                        pe.wait_ge(xT_ready, b + 1)
                        for k in range(KC):
                            last = nc.tensor.transpose(tps[:, k // 3, (k % 3) * P:(k % 3 + 1) * P],
                                                       xn[sl][:, k * P:(k + 1) * P], ident[:, :])
                        last.then_inc(xT_ps, 1)
                        pe.wait_ge(xT_ready, b + 2)
                        pe.wait_ge(al_ready, b + 1)
                        for k in range(KC):
                            last = nc.tensor.matmul(mps[:, 0, 0:2 * H], xT[sl][:, k, :], wa[:, k, 0:2 * H],
                                                    start=(k == 0), stop=(k == KC - 1))
                        last.then_inc(al_ps, 1)
                    blocks(pe, body)

                @block.scalar
                def _(act):
                    act.sem_inc(xT_ready, 1)
                    act.sem_inc(al_ready, 1)

                    def exps(b, sl):
                        act.wait_ge(min_ready, b + 1)
                        nc.scalar.activation(xn[sl], xn[sl], ACT.Exp).then_inc(exp_ready, 1)

                    def body(b, sl, n):
                        act.wait_ge(xT_ps, b + 3)
                        act.wait_ge(copied, b + 1)
                        act.wait_ge(al_ps, b + 1)
                        nc.scalar.activation(xT[sl].rearrange("p (a k) n -> p a (k n)", a=2), tps[:, :, 0:3 * P],
                                             ACT.Copy).then_inc(xT_ready, 1)
                        act.wait_ge(al_ps, b + 3)
                        act.sem_inc(tick_a, 1)
                        nc.scalar.activation(al_node[:, ds(b, 1), 0:2 * H].rearrange("p a h -> p (a h)"),
                                             mps[:, 0, 0:2 * H], ACT.Copy).then_inc(al_ready, 1)
                    act.sem_inc(al_ps, 2)
                    if l == 0:
                        blocks(act, body)
                    else:
                        exps(0, 0)
                        n = NB // 2
                        with act.Fori(0, n) as i:
                            exps(i * 2 + 1, 1)
                            body(i * 2, 0, i)
                            exps(i * 2 + 2, 0)
                            body(i * 2 + 1, 1, i)
                        body(NB - 1, 0, n)

                @block.gpsimd
                def _(pool):
                    pool.sem_inc(copied, 2)

                    def body(b, sl, n):
                        pool.wait_ge(xT_ready, b + 2)
                        pool.sem_inc(tick_p, 1)
                        nc.gpsimd.tensor_copy(featT[:, :, ds(b * P, P)], xT[sl]).then_inc(copied, 1)
                    blocks(pool, body)

        def values(j, H):
            return edges[:, j * NT * 8:j * NT * 8 + NT * H].rearrange("p (t h) -> p t h", h=H)

        def transform(l):
            H = HEADS[l]
            CH = C // H
            L = f"_t{l}"
            slot_ready, mm_done, row_ready, stored = (sem(n + L) for n in ("slot_ready", "mm_done", "row_ready", "stored"))
            tick_a, tick_p, tick_v, chain_p, chain_v = (sem(n + L) for n in ("tick_a", "tick_p", "tick_v", "pool", "dve"))
            st_out, ones_set, idx_ready = sem("st_out" + L), sem("ones_set" + L), sem("idx_ready" + L)
            sc_in, sc_used = [sem(f"sc_in{h}" + L) for h in range(2)], sem("sc_used" + L)
            dst_in, zero_set, zero_st = sem("dst_in" + L), sem("zero_set" + L), sem("zero_st" + L)
            hot_ready, hot_used, cnt_done, cnt_ready, pre_done = (sem(n + L) for n in ("hot", "hot_used", "cnt", "cnt_r", "pre"))
            has_ready, row_ps, tri_set = sem("has" + L), sem("row_ps" + L), sem("tri" + L)
            EW = NT * 8
            at = [EW]

            def spot(n):
                at[0] += n
                assert at[0] <= 4 * EW
                return edges[:, at[0] - n:at[0]]
            cur, prev, nxt, dt_i, lo_i, hi_i, pb_i = (spot(NT).bitcast(i32) for _ in range(7))
            lo_f, hi_f = spot(NT), spot(NT)
            hot_lo = [spot(UN * P // 2).bitcast(bf16).rearrange("p (t n) -> p t n", t=UN) for _ in range(2)]
            hot_hi = [spot(UN * 32 // 2).bitcast(bf16).rearrange("p (t n) -> p t n", t=UN) for _ in range(2)]
            tri, ones = spot(P), spot(P)
            zero_row = ring[:, 0:NT * H]

            with nc.Block() as block:
                @block.sync
                def _(sp):
                    if l == 0:
                        flat = io["dst_halo"]
                        for dst, off in ((prev, 0), (cur, 1), (nxt, 2)):
                            sp.dma_start(dst, flat[off:off + EP].rearrange("(p t) -> p t", p=P)).then_inc(dst_in, 16)
                        sp.dma_start(dt_i, io["dst_t"]).then_inc(dst_in, 16)
                        sp.dma_start(pb_i, io["dst_last"][0, 0:NT].partition_broadcast(P)).then_inc(dst_in, 16)
                    sp.wait_ge(zero_set, 1)
                    sp.dma_start(first_val[l].rearrange("(p t) h -> p (t h)", p=P), zero_row).then_inc(zero_st, 16)
                    sp.sem_inc(stored, 2)

                    def body(b, sl, n):
                        sp.wait_ge(row_ready, b + 3)
                        sp.dma_start(feat_tab[l][ds(b * P, P), :], raw[sl]).then_inc(st_out, 16)
                        sp.wait_ge(st_out, b * 16 + 16)
                        sp.sem_inc(stored, 1)
                    blocks(sp, body)
                    sp.wait_ge(zero_st, 16)

                @block.scalar
                def _(act):
                    act.sem_inc(mm_done, 2)
                    act.sem_inc(row_ready, 2)
                    act.wait_ge(ones_set, 1)

                    def slot(b, sl):
                        act.wait_ge(mm_done, b + 1)
                        act.sem_inc(tick_a, 1)
                        nc.scalar.activation(xT[sl], featT[:, :, ds(b * P, P)], ACT.Copy).then_inc(slot_ready, 1)

                    def body(b, sl, n):
                        act.wait_ge(mm_done, b + 3)
                        act.wait_ge(stored, b + 1)
                        for c in range(2):
                            if l == 0:
                                dst = raw[sl].rearrange("p (h c) -> p h c", h=H)[:, c * 4:c * 4 + 4, 0:CH]
                                src = acc[:, 2 * sl + c, 0:C // 2].rearrange("p (h c) -> p h c", c=CH)
                            else:
                                dst, src = raw[sl][:, c * (C // 2):(c + 1) * (C // 2)], acc[:, 2 * sl + c, 0:C // 2]
                            ins = nc.scalar.activation(dst, src, ACT.Copy)
                        ins.then_inc(row_ready, 1)
                    slot(0, 0)
                    n = NB // 2
                    with act.Fori(0, n) as i:
                        slot(i * 2 + 1, 1)
                        body(i * 2, 0, i)
                        slot(i * 2 + 2, 0)
                        body(i * 2 + 1, 1, i)
                    body(NB - 1, 0, n)

                @block.tensor
                def _(pe):
                    if l == 0:
                        for j in range(3):
                            if j == 0:
                                pe.wait_ge(has_ready, 1)
                            nc.tensor.transpose(mps[0:8, j // 2, (j % 2) * P:(j % 2 + 1) * P], has[:, j, :],
                                                ident[:, :]).then_inc(row_ps, 1)

                        def hist(i, first, last):
                            for j in range(2):
                                pe.wait_ge(hot_ready, i * 2 + j + 1)
                                for t in range(UN):
                                    m = nc.tensor.matmul(tps[:, 0, 0:NB], hot_lo[j][:, t, :], hot_hi[j][:, t, 0:NB],
                                                         start=first and j + t == 0, stop=last and j == 1 and t == UN - 1)
                                m.then_inc(hot_used, 1)
                        pe.sem_inc(hot_used, 2)
                        hist(0, True, False)
                        with pe.Fori(1, TURNS // 2 - 1) as i:
                            hist(i, False, False)
                        hist(TURNS // 2 - 1, False, True)
                        pe.wait_ge(tri_set, 2)
                        pe.wait_ge(cnt_ready, 1)
                        nc.tensor.matmul(mps[:, 0, 0:NB], tri, small[:, 0, :], start=True, stop=True)
                        nc.tensor.matmul(mps[:, 1, 0:NB], ones, small[:, 0, :], start=True, stop=True).then_inc(pre_done, 1)

                    def body(b, sl, n):
                        pe.wait_ge(slot_ready, b + 1)
                        pe.wait_ge(row_ready, b + 1)
                        for k in range(KC):
                            for c in range(2):
                                m = nc.tensor.matmul(acc[:, 2 * sl + c, 0:C // 2], xT[sl][:, k, :],
                                                     wg[:, k, c * (C // 2):(c + 1) * (C // 2)],
                                                     start=(k == 0), stop=(k == KC - 1))
                        m.then_inc(mm_done, 1)
                    blocks(pe, body)

                @block.gpsimd
                def _(pool):
                    st = Steps(pool, chain_p)
                    nc.gpsimd.memset(zero_row, 0.0).then_inc(zero_set, 1)
                    if l == 0:
                        st.step(nc.gpsimd.memset(tri, 1.0))
                        nc.gpsimd.affine_select(out=tri, in_=tri, compare_op=ALU.is_gt, fill=0.0, base=0,
                                                pattern=[[1, P]], channel_multiplier=-1).then_inc(tri_set, 1)
                        nc.gpsimd.memset(ones, 1.0).then_inc(tri_set, 1)
                    pool.sem_inc(sc_used, 2)
                    with pool.Fori(0, TURNS) as i:
                        st.loop(i, 2)
                        for h in range(2):
                            pool.wait_ge(sc_used, i * 2 + h + 1)
                            pool.sem_inc(tick_p, 1)
                            st.step(nc.gpsimd.tensor_copy(islot[:, h, :], src_p[:, ds(i * UN + h * RING, RING)]), tick_p)
                            for k in range(RING):
                                pool.indirect_dma_start(sg[:, h, k * H:(k + 1) * H], None, score_tab[l],
                                                        bass.IndirectOffsetOnAxis(ap=islot[:, h, k:k + 1], axis=0)
                                                        ).then_inc(sc_in[h], 16)
                    st.done(TURNS)

                @block.vector
                def _(dve):
                    st = Steps(dve, chain_v)
                    V = nc.vector
                    V.memset(raw[0], 1.0)
                    V.memset(raw[1], 1.0).then_inc(ones_set, 1)

                    def scores(i, h):
                        dve.wait_ge(sc_in[h], (i + 1) * (RING * 16))
                        dve.sem_inc(tick_v, 1)
                        V.tensor_copy(edges[:, ds((i * UN + h * RING) * H, RING * H)], sg[:, h, 0:RING * H]).then_inc(sc_used, 1)
                    if l == 1:
                        with dve.Fori(0, TURNS) as i:
                            scores(i, 0)
                            scores(i, 1)
                        return
                    dve.wait_ge(dst_in, 80)
                    V.memset(row_scan[:, 2, :], 0.0)
                    V.memset(row_scan[:, 0:2, :], NEG)
                    V.tensor_single_scalar(bend[:, :], bend[:, :], 7, ALU.logical_shift_right)
                    V.tensor_tensor(rst_f[:, :], cur, prev, ALU.not_equal)
                    st.step(V.tensor_tensor(rst_b[:, :], cur, nxt, ALU.not_equal))
                    V.tensor_reduce(small[:, 1, 0:1], rst_f[:, :], AX, ALU.max)
                    V.tensor_scalar(keep[:, :], rst_f[:, :], -1.0, 1.0, ALU.mult, ALU.add)
                    st.step(V.tensor_reduce(small[:, 1, 1:2], rst_b[:, :], AX, ALU.max))
                    V.tensor_scalar(rst_f[:, :], rst_f[:, :], NEG, None, ALU.mult)
                    V.tensor_scalar(rst_b[:, :], rst_b[:, :], NEG, None, ALU.mult)
                    V.tensor_scalar(has[:, 0, :], small[:, 1, 0:1].to_broadcast([P, 8]), NEG, None, ALU.mult)
                    V.tensor_scalar(has[:, 1, :], small[:, 1, 1:2].to_broadcast([P, 8]), NEG, None, ALU.mult)
                    V.tensor_scalar(has[:, 2, :], small[:, 1, 0:1].to_broadcast([P, 8]), -1.0, 1.0, ALU.mult,
                                    ALU.add).then_inc(has_ready, 1)
                    V.tensor_single_scalar(lo_i, dt_i, P - 1, ALU.bitwise_and)
                    V.tensor_single_scalar(hi_i, dt_i, 7, ALU.logical_shift_right)
                    st.step(V.tensor_single_scalar(pb_i, pb_i, 7, ALU.logical_shift_right))
                    V.tensor_copy(lo_f, lo_i)
                    V.tensor_copy(hi_f, hi_i)
                    V.tensor_copy(dst_t[:, :], dt_i)
                    st.step(V.tensor_scalar(dst_rel[:, :], pb_i, float(-P), None, ALU.mult))
                    st.step(V.tensor_tensor(dst_rel[:, :], dst_rel[:, :], dst_t[:, :], ALU.add))
                    dve.wait_ge(row_ps, 3)
                    for j in range(3):
                        V.tensor_copy(row_rst[:, j, :], mps[0:8, j // 2, (j % 2) * P:(j % 2 + 1) * P])
                    with dve.Fori(0, TURNS // 2) as i:
                        for j in range(2):
                            t = i * 2 + j
                            dve.wait_ge(hot_used, t + 1)
                            dve.sem_inc(tick_v, 1)
                            for hot, val, w in ((hot_lo[j], lo_f, P), (hot_hi[j], hi_f, 32)):
                                ins = V.tensor_tensor(hot, iota_f[:, 0:w].unsqueeze(1).to_broadcast([P, UN, w]),
                                                      val[:, ds(t * UN, UN)].unsqueeze(2).to_broadcast([P, UN, w]), ALU.is_equal)
                            ins.then_inc(hot_ready, 1)
                            scores(t, 0)
                            scores(t, 1)
                    dve.wait_ge(hot_used, TURNS + 2)
                    st.step(V.tensor_copy(small[:, 0, :], tps[:, 0, 0:NB]))
                    dve.sem_inc(cnt_ready, 1)
                    V.memset(small[:, 4, :], 1.0)
                    dve.wait_ge(pre_done, 1)
                    st.step(V.tensor_copy(small[:, 1, :], mps[:, 1, 0:NB]))
                    st.step(V.tensor_tensor_scan(small[:, 2, :], small[:, 4, :], small[:, 1, :], 0.0, ALU.mult, ALU.add))
                    st.step(V.tensor_tensor(small[:, 2, :], small[:, 2, :], small[:, 1, :], ALU.subtract))
                    st.step(V.tensor_tensor(small[:, 2, :], small[:, 2, :], mps[:, 0, 0:NB], ALU.add))
                    st.step(V.tensor_scalar(small[:, 3, :], small[:, 0, :], 0.0, 1e6, ALU.is_equal, ALU.mult))
                    st.step(V.tensor_tensor(first_idx[:, :], small[:, 2, :], small[:, 3, :], ALU.add))

        def scores(l):
            H = HEADS[l]
            L = f"_s{l}"
            first_st, first_in, ex_ready, ex_st, ex_in, exT_ps, exT_ready = (
                sem(n + L) for n in ("first_st", "first_in", "ex_ready", "ex_st", "ex_in", "exT_ps", "exT_ready"))
            last_ready, row_ps, row_done, carry_ps, chain_v, d_ready = (
                sem(n + L) for n in ("last", "row_ps", "row_done", "carry_ps", "dve", "d_ready"))
            src_s, fwd, top, dst_s = (values(j, H) for j in range(4))
            rows = ring[:, 0:4 * P * H].rearrange("p (c n) -> p c n", c=4)
            R = NT // 4
            with nc.Block() as block:
                @block.gpsimd
                def _(pool):
                    for b in range(NB):
                        pool.indirect_dma_start(first_val[l], bass.IndirectOffsetOnAxis(ap=first_idx[:, b:b + 1], axis=0),
                                                al_node[:, b, H:2 * H], None, bounds_check=EP - 1,
                                                oob_is_err=False).then_inc(first_st, 16)

                @block.sync
                def _(sp):
                    sp.wait_ge(first_st, 16 * NB)
                    sp.dma_start(dst_s, first_val[l].rearrange("(p t) h -> p t h", p=P)).then_inc(first_in, 16)
                    sp.wait_ge(ex_ready, 1)
                    sp.dma_start(edge_ex[l].rearrange("(p t) h -> p t h", p=P), src_s).then_inc(ex_st, 16)
                    sp.wait_ge(ex_st, 16)
                    sp.dma_start(rows[0:R, :, :], edge_ex[l].rearrange("(c r q) h -> r c (q h)", c=4, q=P)).then_inc(ex_in, 16)

                @block.tensor
                def _(pe):
                    for n, j in enumerate((1, 2, 1)):
                        pe.wait_ge(last_ready, n + 1)
                        nc.tensor.transpose(mps[0:H, 0, 0:P], values(j, H)[:, 0 if n == 1 else NT - 1, :],
                                            ident[:, :]).then_inc(row_ps, 1)
                        pe.wait_ge(row_done, n + 1)
                        src = row_scan[0:H, n, 1:P + 1] if n == 1 else row_scan[0:H, n, 0:P]
                        nc.tensor.transpose(mps[:, 1, 0:H], src, ident[0:H, 0:H]).then_inc(carry_ps, 1)
                    pe.wait_ge(ex_in, 16)
                    for h in range(H):
                        if h > 1:
                            pe.wait_ge(exT_ready, h - 1)
                        for c in range(4):
                            m = nc.tensor.transpose(tps[:, h % 2, c * R:(c + 1) * R],
                                                    rows[0:R, c, :].rearrange("r (q h) -> r q h", h=H)[:, :, h],
                                                    ident[0:R, 0:R])
                        m.then_inc(exT_ps, 1)

                @block.scalar
                def _(act):
                    act.wait_ge(d_ready, 1)
                    nc.scalar.activation(src_s, src_s, ACT.Exp).then_inc(ex_ready, 1)
                    for h in range(H):
                        act.wait_ge(exT_ps, h + 1)
                        nc.scalar.activation(fwd[:, :, h], tps[:, h % 2, 0:NT], ACT.Copy).then_inc(exT_ready, 1)

                @block.vector
                def _(dve):
                    st = Steps(dve, chain_v)
                    V = nc.vector

                    def scan(out_j, in_j, reset, init, ops, back):
                        for h in range(H):
                            o, r, x = values(out_j, H)[:, :, h], reset[:, :], values(in_j, H)[:, :, h]
                            if back:
                                o, r, x = o[:, ::-1], r[:, ::-1], x[:, ::-1]
                            ins = V.tensor_tensor_scan(o, r, x, init if isinstance(init, float) else init[:, h:h + 1], *ops)
                        st.step(ins)

                    def whole_scan(n, out_j, in_j, reset, ops, back, init):
                        scan(out_j, in_j, reset, init, ops, back)
                        dve.sem_inc(last_ready, 1)
                        dve.wait_ge(row_ps, n + 1)
                        o, r, x = row_scan[0:H, n, 0:P] if back else row_scan[0:H, n, 1:P + 1], row_rst[0:H, n, :], mps[0:H, 0, 0:P]
                        if back:
                            o, r, x = o[:, ::-1], r[:, ::-1], x[:, ::-1]
                        V.tensor_tensor_scan(o, r, x, init, *ops).then_inc(row_done, 1)
                        dve.wait_ge(carry_ps, n + 1)
                        st.step(V.tensor_copy(carry[:, n, 0:H], mps[:, 1, 0:H]))
                        scan(out_j, in_j, reset, carry[:, n, :], ops, back)
                    peak, hold = (ALU.add, ALU.max), (ALU.mult, ALU.add)
                    whole_scan(0, 1, 0, rst_f, peak, False, NEG)
                    whole_scan(1, 2, 1, rst_b, peak, True, NEG)
                    dve.wait_ge(first_in, 16)
                    whole_scan(2, 1, 3, keep, hold, False, 0.0)
                    st.step(V.tensor_tensor(src_s, src_s, fwd, ALU.add))
                    st.step(V.tensor_tensor(top, top, fwd, ALU.add))
                    st.step(V.scalar_tensor_tensor(src_s, src_s, SLOPE, src_s, ALU.mult, ALU.max))
                    st.step(V.scalar_tensor_tensor(top, top, SLOPE, top, ALU.mult, ALU.max))
                    V.tensor_tensor(src_s, src_s, top, ALU.subtract).then_inc(d_ready, 1)

        def aggregate(l):
            H = HEADS[l]
            L = f"_a{l}"
            row_in = [sem(f"row_in{k}" + L) for k in range(RING)]
            msg_ready, hot_ready, open_ready, tile_mm, open_mm = (
                sem(n + L) for n in ("msg", "hot", "open_hot", "tile_mm", "open_mm"))
            flushed, st_out, stored, zero_set = (sem(n + L) for n in ("flushed", "st_out", "stored", "zero_set"))
            tick_a, tick_p, chain_p, chain_v = (sem(n + L) for n in ("tick_a", "tick_p", "pool", "dve"))
            ex = values(1, H)
            rows = [ring[:, k * ROW:(k + 1) * ROW] for k in range(RING)]

            unit_in, unit_used, scale_in, chain_x = sem("unit_in" + L), sem("unit_used" + L), sem("scale_in" + L), sem("open_dve" + L)
            slow, hebb = (v.rearrange("p k n -> p (k n)") for v in xT)
            scales = wg[:, 0, 0:4 * UNITS]

            def open_blocks(eng, t):
                b0 = eng.value_load(bend[0:1, ds(t, 1)], min_val=0, max_val=NB - 1)
                b1 = eng.value_load(bend[0:1, ds(t + 1, 1)], min_val=0, max_val=NB - 1)
                return b0, b1

            with nc.Block() as block:
                @block.gpsimd
                def _(pool):
                    st = Steps(pool, chain_p)
                    nc.gpsimd.memset(zeros, 0.0).then_inc(zero_set, 1)
                    pool.sem_inc(tile_mm, RING)
                    with pool.Fori(0, TURNS) as i:
                        st.loop(i, 2)
                        for u in range(UN):
                            t = i * UN + u
                            k = u % RING
                            if k == 0:
                                h = u // RING
                                st.step(nc.gpsimd.tensor_copy(islot[:, h, :], src_t[:, ds(t, RING)]), tick_p)
                            pool.wait_ge(tile_mm, t + 1)
                            pool.sem_inc(tick_p, 1)
                            if k == 0:
                                last_open = pool.value_load(bend[0:1, ds(t, 1)], min_val=0, max_val=NB - 1)
                                pool.wait_ge(open_mm, last_open + 1)
                                pool.sem_inc(tick_p, 1)
                            pool.indirect_dma_start(rows[k], None, feat_tab[l],
                                                    bass.IndirectOffsetOnAxis(ap=islot[:, u // RING, k:k + 1], axis=0)
                                                    ).then_inc(row_in[k], 16)
                    st.done(TURNS)

                @block.vector
                def _(dve):
                    st = Steps(dve, chain_v)
                    V = nc.vector

                    def combine(j):
                        dve.wait_ge(unit_in, (j + 1) * 48)
                        st.step(V.tensor_tensor(slow.rearrange("p (a n) -> p a n", a=4), slow.rearrange("p (a n) -> p a n", a=4),
                                                scales[:, ds(j * 4, 4)].unsqueeze(2).to_broadcast([P, 4, C // 4]), ALU.mult))
                        st.step(V.tensor_tensor(slow, slow, hebb, ALU.add))
                        V.tensor_tensor(big[:, ds(j * C, C)], big[:, ds(j * C, C)], slow, ALU.add).then_inc(unit_used, 1)

                    def turn(i):
                        for u in range(UN):
                            t = i * UN + u
                            k = u % RING
                            dve.wait_ge(row_in[k], i * 32 + (u // RING + 1) * 16)
                            if l == 0:
                                r3 = rows[k].rearrange("p (h c) -> p h c", h=H)
                                V.tensor_tensor(r3, r3, ex[:, ds(t, 1), :].rearrange("p a h -> p h a").to_broadcast([P, H, ROW // H]),
                                                ALU.mult).then_inc(msg_ready, 1)
                                V.tensor_scalar(onehot[:, k, :], iota_f[:, :], dst_rel[:, ds(t, 1)], None,
                                                ALU.is_equal).then_inc(hot_ready, 1)
                            else:
                                V.tensor_scalar(onehot[:, k, :], iota_f[:, :], dst_rel[:, ds(t, 1)], ex[:, ds(t, 1), 0],
                                                ALU.is_equal, ALU.mult).then_inc(hot_ready, 1)
                            b0, b1 = open_blocks(dve, t)
                            with dve.If(b1 > b0):
                                with dve.Fori(b0 + 1, b1 + 1) as b:
                                    dve.wait_ge(open_mm, b)
                                    ins = V.tensor_scalar(onehot_x, iota_f[:, :], blk_base[:, ds(b, 1)], dst_t[:, ds(t, 1)],
                                                          ALU.subtract, ALU.is_equal)
                                    if l == 1:
                                        ins.then_inc(chain_x, 1)
                                        dve.wait_ge(chain_x, b)
                                        ins = V.tensor_scalar(onehot_x, onehot_x, ex[:, ds(t, 1), 0], None, ALU.mult)
                                    ins.then_inc(open_ready, 1)
                    if l == 0:
                        with dve.Fori(0, TURNS) as i:
                            turn(i)
                    else:
                        dve.wait_ge(scale_in, 16)
                        with dve.Fori(0, UNITS) as i:
                            st.loop(i, 2)
                            turn(i)
                            combine(i)
                        st.done(UNITS)
                        with dve.Fori(UNITS, TURNS) as i:
                            turn(i)

                @block.tensor
                def _(pe):
                    def sums(par, hot, k, start):
                        for c in range(2):
                            m = nc.tensor.matmul(acc[:, ds(par * 2 + c, 1), 0:HALF].rearrange("p a n -> p (a n)"), hot,
                                                 rows[k][:, c * HALF:(c + 1) * HALF], start=start, stop=True, skip_group_check=True)
                        return m
                    pe.wait_ge(zero_set, 1)
                    for c in range(2):
                        m = nc.tensor.matmul(acc[:, c, 0:HALF], zeros[:, 0:P], zeros, start=True, stop=True,
                                             skip_group_check=True)
                    m.then_inc(open_mm, 1)
                    with pe.Fori(0, TURNS) as i:
                        for u in range(UN):
                            t = i * UN + u
                            k = u % RING
                            b0, b1 = open_blocks(pe, t)
                            if l == 0:
                                pe.wait_ge(msg_ready, t + 1)
                            else:
                                pe.wait_ge(row_in[k], i * 32 + (u // RING + 1) * 16)
                            pe.wait_ge(hot_ready, t + 1)
                            sums(b0 % 2, onehot[:, k, :], k, False).then_inc(tile_mm, 1)
                            with pe.If(b1 > b0):
                                with pe.Fori(b0 + 1, b1 + 1) as b:
                                    pe.wait_ge(open_ready, b)
                                    pe.wait_ge(flushed, b)
                                    sums(b % 2, onehot_x, k, True).then_inc(open_mm, 1)
                    for c in range(2):
                        m = nc.tensor.matmul(acc[:, 2 * ((NB - 1) % 2) + c, 0:HALF], zeros[:, 0:P], zeros,
                                             start=False, stop=True, skip_group_check=True)
                    m.then_inc(open_mm, 1)

                @block.scalar
                def _(act):
                    act.sem_inc(flushed, 1)

                    def body(b, sl, n):
                        act.wait_ge(open_mm, b + 2)
                        nc.scalar.activation(raw[sl].rearrange("p (a n) -> p a n", a=2), acc[:, 2 * sl:2 * sl + 2, 0:HALF],
                                             ACT.Copy).then_inc(flushed, 1)
                        act.wait_ge(flushed, b + 2)
                        act.dma_start(agg_raw[l][ds(b * P, P), :], raw[sl]).then_inc(st_out, 16)
                        act.wait_ge(st_out, b * 16 + 16)
                    blocks(act, body)

                if l == 1:
                    @block.sync
                    def _(sp):
                        sp.dma_start(scales, io["w_scale"]).then_inc(scale_in, 16)
                        sp.sem_inc(unit_used, 1)
                        with sp.Fori(0, UNITS) as j:
                            sp.wait_ge(unit_used, j + 1)
                            sp.dma_start(big[:, ds(j * C, C)], io["w_fast"][ds(j, 1), :, :].rearrange("a p n -> (a p) n")).then_inc(unit_in, 16)
                            sp.dma_start(slow, io["w_slow"][ds(j, 1), :, :].rearrange("a p n -> (a p) n")).then_inc(unit_in, 16)
                            sp.dma_start(hebb, io["w_hebb"][ds(j, 1), :, :].rearrange("a p n -> (a p) n")).then_inc(unit_in, 16)

        wgf = wg[:, :, :].rearrange("p k n -> p (k n)")
        gatesT = wgf[0:NE, 0:NP]
        b2_rows = wgf[0:NE, NP:NP + C]
        rcol = NP + C
        gain, const8, b1col = wgf[:, rcol:rcol + NE], wgf[:, rcol + NE:rcol + 2 * NE], wgf[:, rcol + 16:rcol + 16 + HK]
        rw = wgf[:, rcol + 32:rcol + 32 + KC * RW].rearrange("p (k n) -> p k n", k=KC)
        pick = ring[0:NE, 5 * SUP:5 * SUP + HK * P].rearrange("p (k n) -> p k n", k=HK)

        def route():
            L = "_r"
            const_in, in_ld, x_in = sem("const_in" + L), [sem(f"in{j}" + L) for j in range(2)], [sem(f"x_in{j}" + L) for j in range(2)]
            bias_added, sq_in, sq_out, x1_ready, xn_ready, xT_ps, xT_ready, rt_ps, rt_ready = (
                sem(n + L) for n in ("bias_added", "sq_in", "sq_out", "x1_ready", "xn_ready", "xT_ps", "xT_ready", "rt_ps", "rt_ready"))
            chain_v, tick_a, tick_v, tick_p, st_out, k_ready, k_ps, one_ready = (
                sem(n + L) for n in ("dve", "tick_a", "tick_v", "tick_p", "st_out", "k_ready", "k_ps", "one_ready"))
            g_sq, g_rt, g_d, g_e, g_ready, g_ps, emb_sq, emb_rt, emb_ready = (
                sem(n + L) for n in ("g_sq", "g_rt", "g_d", "g_e", "g_ready", "g_ps", "emb_sq", "emb_rt", "emb_ready"))
            at = [0]

            def spot(n):
                at[0] += n
                assert at[0] <= 4 * NT * 8
                return edges[:, at[0] - n:at[0]]
            bias, emb_all, emb_tmp, emb8, probe, embT = spot(C), spot(NE * DR), spot(NE * DR), spot(DR), spot(C), spot(NE)
            fat, norm8, n8 = spot(NE), spot(NE), spot(8)
            logits = spot(NB * RW).rearrange("p (b n) -> p b n", b=NB)
            v3 = [spot(NB * NE).rearrange("p (b n) -> p b n", b=NB) for _ in range(5)]
            sqp = spot(NB * DR).rearrange("p (b n) -> p b n", b=NB)
            v1 = [spot(NB) for _ in range(4)]
            idx = spot(NB * NE).bitcast(u32).rearrange("p (b n) -> p b n", b=NB)
            st2 = [spot(2) for _ in range(2)]
            banks = [acc[0:NE, j, :] for j in range(4)] + [tps[0:NE, j, :] for j in range(2)] + [mps[0:NE, 0, :]]

            with nc.Block() as block:
                @block.sync
                def _(sp):
                    for dst, src in ((bias, io["b2g"].partition_broadcast(P)), (emb_all, io["emb"].rearrange("a b -> (a b)").partition_broadcast(P)),
                                     (emb8[0:NE, :], io["emb"]), (probe[0:DR, :], io["probe_w"]),
                                     (fat, io["fatigue"].partition_broadcast(P)), (const8, io["energy"].partition_broadcast(P)),
                                     (rw[:, :, 0:NE + DR], io["route_wT"].rearrange("(k p) n -> p k n", p=P)),
                                     (b1col, io["b1_col"]), (b2_rows, io["b2_rows"])):
                        sp.dma_start(dst, src).then_inc(const_in, 16)

                    def load(b, sl):
                        sp.dma_start(raw[sl], agg_raw[1][ds(b * P, P), :]).then_inc(in_ld[sl], 16)
                        sp.dma_start(tmp[sl], io["x"][ds(b * P, P), :]).then_inc(x_in[sl], 16)

                    def store(b, sl):
                        sp.wait_ge(x1_ready, b + 1)
                        sp.dma_start(mid_rows[ds(b * P, P), :], tmp[sl]).then_inc(st_out, 16)
                        sp.wait_ge(xT_ready, b + 2)
                        sp.dma_start(mid_featT[ds(b, 1), :, :].rearrange("a p n -> (a p) n"),
                                     xT[sl].rearrange("p k n -> p (k n)")).then_inc(st_out, 16)
                        sp.wait_ge(st_out, b * 32 + 32)
                        sp.sem_inc(one_ready, 1)
                    for sl in range(2):
                        load(sl, sl)

                    def body(b, sl, n):
                        store(b, sl)
                        load(b + 2, sl)
                    blocks(sp, body, last=NB - 2)
                    for b in (NB - 2, NB - 1):
                        store(b, b % 2)

                @block.gpsimd
                def _(pool):
                    nc.gpsimd.memset(rw[:, :, RW - 1:RW], 1.0 / C)
                    pool.wait_ge(const_in, 16 * 9)

                    def body(b, sl, n):
                        pool.wait_ge(x_in[sl], n * 16 + 16)
                        nc.gpsimd.tensor_tensor(tmp[sl], tmp[sl], bias, ALU.add).then_inc(bias_added, 1)
                    blocks(pool, body)
                    st = Steps(pool, tick_p)
                    st.step(nc.gpsimd.memset(pick, 1.0))
                    st.step(nc.gpsimd.affine_select(out=pick, in_=pick, compare_op=ALU.is_ge, fill=0.0, base=0,
                                                    pattern=[[P, HK], [1, P]], channel_multiplier=-HID))
                    nc.gpsimd.affine_select(out=pick, in_=pick, compare_op=ALU.is_ge, fill=0.0, base=HID - 1,
                                            pattern=[[-P, HK], [-1, P]], channel_multiplier=HID)

                @block.tensor
                def _(pe):
                    pe.wait_ge(emb_ready, 1)
                    nc.tensor.transpose(mps[0:DR, 0, 0:NE], emb8[0:NE, :], ident[0:NE, 0:NE]).then_inc(k_ps, 1)
                    pe.wait_ge(emb_ready, 2)
                    for k in range(KC):
                        m = nc.tensor.matmul(mps[:, 1, k * NE:(k + 1) * NE], probe[0:DR, k * P:(k + 1) * P], embT[0:DR, :],
                                             start=True, stop=True)
                    m.then_inc(k_ps, 1)
                    pe.wait_ge(k_ready, 1)
                    pe.sem_inc(xT_ps, 2)

                    def body(b, sl, n):
                        pe.wait_ge(xn_ready, b + 1)
                        pe.wait_ge(xT_ready, b + 1)
                        for k in range(KC):
                            m = nc.tensor.transpose(tps[:, k // 3, (k % 3) * P:(k % 3 + 1) * P],
                                                    xn[sl][:, k * P:(k + 1) * P], ident[:, :])
                        m.then_inc(xT_ps, 1)
                        pe.wait_ge(xT_ready, b + 2)
                        pe.wait_ge(rt_ready, b + 1)
                        for k in range(KC):
                            m = nc.tensor.matmul(mps[:, 0, 0:RW], xT[sl][:, k, :], rw[:, k, :], start=(k == 0), stop=(k == KC - 1))
                        m.then_inc(rt_ps, 1)
                    blocks(pe, body)
                    pe.wait_ge(g_ready, 1)
                    pe.wait_ge(rt_ready, NB + 1)
                    for b in range(NB):
                        nc.tensor.transpose(banks[b // 4][:, (b % 4) * P:(b % 4 + 1) * P], v3[0][:, b, :], ident[:, :]
                                            ).then_inc(g_ps, 1)

                @block.scalar
                def _(act):
                    act.wait_ge(emb_sq, 1)
                    nc.scalar.activation(norm8, norm8, ACT.Sqrt)
                    nc.scalar.activation(n8[0:NE, 0:1], n8[0:NE, 0:1], ACT.Sqrt).then_inc(emb_rt, 1)
                    act.sem_inc(xT_ready, 1)
                    act.sem_inc(rt_ready, 1)
                    act.sem_inc(one_ready, 2)

                    def roots(b, sl):
                        act.wait_ge(sq_in, b + 1)
                        nc.scalar.activation(st2[sl][:, 1:2], st2[sl][:, 1:2], ACT.Sqrt).then_inc(sq_out, 1)

                    def body(b, sl, n):
                        act.wait_ge(xT_ps, b + 3)
                        act.wait_ge(one_ready, b + 1)
                        act.wait_ge(rt_ps, b + 1)
                        nc.scalar.activation(xT[sl].rearrange("p (a k) n -> p a (k n)", a=2), tps[:, :, 0:3 * P],
                                             ACT.Copy).then_inc(xT_ready, 1)
                        act.wait_ge(rt_ps, b + 3)
                        act.sem_inc(tick_a, 1)
                        nc.scalar.activation(logits[:, ds(b, 1), :].rearrange("p a n -> p (a n)"), mps[:, 0, 0:RW],
                                             ACT.Copy).then_inc(rt_ready, 1)
                    act.sem_inc(rt_ps, 2)
                    roots(0, 0)
                    n = NB // 2
                    with act.Fori(0, n) as i:
                        roots(i * 2 + 1, 1)
                        body(i * 2, 0, i)
                        roots(i * 2 + 2, 0)
                        body(i * 2 + 1, 1, i)
                    body(NB - 1, 0, n)
                    act.wait_ge(g_sq, 1)
                    nc.scalar.activation(v1[0], v1[0], ACT.Sqrt).then_inc(g_rt, 1)
                    act.wait_ge(g_d, 1)
                    nc.scalar.activation(v1[1], v1[1], ACT.Exp).then_inc(g_e, 1)
                    for j in range(7):
                        w = min(4 * P, NP - 4 * P * j)
                        act.wait_ge(g_ps, min(4 * j + 4, NB))
                        nc.scalar.activation(gatesT[:, 4 * P * j:4 * P * j + w], banks[j][:, 0:w], ACT.Copy)

                @block.vector
                def _(dve):
                    st = Steps(dve, chain_v)
                    V = nc.vector
                    dve.wait_ge(const_in, 16 * 9)
                    st.step(V.tensor_tensor(emb_tmp, emb_all, emb_all, ALU.mult))
                    V.tensor_reduce(norm8, emb_tmp.rearrange("p (e d) -> p e d", e=NE), AX, ALU.add)
                    st.step(V.tensor_tensor(sqp[0:NE, 0, :], emb8[0:NE, :], emb8[0:NE, :], ALU.mult))
                    V.tensor_reduce(n8[0:NE, 0:1], sqp[0:NE, 0, :], AX, ALU.add).then_inc(emb_sq, 1)
                    st.step(V.tensor_scalar(fat, fat, -0.1, None, ALU.mult))
                    st.step(V.scalar_tensor_tensor(const8, const8, 0.1, fat, ALU.mult, ALU.add))
                    dve.wait_ge(emb_rt, 1)
                    V.tensor_scalar(gain, norm8, 0.02, 0.02, ALU.mult, ALU.add)
                    st.step(V.tensor_scalar_max(n8[0:NE, 0:1], n8[0:NE, 0:1], 1e-12))
                    st.step(V.reciprocal(n8[0:NE, 0:1], n8[0:NE, 0:1]))
                    V.tensor_scalar(emb8[0:NE, :], emb8[0:NE, :], n8[0:NE, 0:1], 0.02, ALU.mult, ALU.mult).then_inc(emb_ready, 1)
                    dve.wait_ge(k_ps, 1)
                    V.tensor_copy(embT[0:DR, :], mps[0:DR, 0, 0:NE]).then_inc(emb_ready, 1)
                    dve.wait_ge(k_ps, 2)
                    V.tensor_copy(rw[:, :, NE + DR:RW - 1], mps[:, 1, 0:KC * NE].rearrange("p (k e) -> p k e", k=KC)
                                  ).then_inc(k_ready, 1)

                    def first_half(b, sl, n):
                        z = raw[sl][:, C:C + 1]
                        dve.wait_ge(in_ld[sl], n * 16 + 16)
                        st.step(V.tensor_scalar_add(z, z, 1e-16))
                        st.step(V.reciprocal(z, z))
                        dve.wait_ge(bias_added, b + 1)
                        st.step(V.scalar_tensor_tensor(tmp[sl], raw[sl][:, 0:C], z, tmp[sl], ALU.mult, ALU.add))
                        dve.sem_inc(x1_ready, 1)
                        V.bn_stats(stats[:, 0:6], tmp[sl][:, 0:C // 2])
                        st.step(V.bn_stats(stats[:, 6:12], tmp[sl][:, C // 2:C]), tick_v)
                        st.step(V.bn_aggr(st2[sl], stats[:, :]))
                        V.tensor_scalar_add(st2[sl][:, 1:2], st2[sl][:, 1:2], LN_EPS).then_inc(sq_in, 1)

                    def second_half(b, sl):
                        dve.wait_ge(sq_out, b + 1)
                        st.step(V.reciprocal(st2[sl][:, 1:2], st2[sl][:, 1:2]))
                        dve.wait_ge(xT_ps, b + 1)
                        V.tensor_scalar(xn[sl], tmp[sl], st2[sl][:, 0:1], st2[sl][:, 1:2], ALU.subtract,
                                        ALU.mult).then_inc(xn_ready, 1)
                    first_half(0, 0, 0)

                    def body(b, sl, n):
                        first_half(b, sl, n)
                        second_half(b - 1, 1 - sl)
                    blocks(dve, body, st, 6, first=1)
                    second_half(NB - 1, 0)
                    dve.wait_ge(rt_ready, NB + 1)
                    A, pr, B, mean = logits[:, :, 0:NE], logits[:, :, NE:NE + DR], logits[:, :, NE + DR:RW - 1], logits[:, :, RW - 1]
                    wide = lambda v: v.unsqueeze(2).to_broadcast([P, NB, NE])
                    row = lambda v: v.unsqueeze(1).to_broadcast([P, NB, NE])
                    st.step(V.tensor_tensor(sqp, pr, pr, ALU.mult))
                    V.tensor_reduce(v1[0], sqp, AX, ALU.add).then_inc(g_sq, 1)
                    st.step(V.tensor_tensor(v3[0], A, row(const8), ALU.add))
                    st.step(V.tensor_tensor(v3[1], row(gain), wide(mean), ALU.mult))
                    st.step(V.tensor_tensor(v3[0], v3[0], v3[1], ALU.add))
                    dve.wait_ge(g_rt, 1)
                    st.step(V.tensor_scalar_max(v1[0], v1[0], 1e-12))
                    st.step(V.reciprocal(v1[0], v1[0]))
                    st.step(V.tensor_tensor(v3[1], B, wide(v1[0]), ALU.mult))
                    st.step(V.tensor_tensor(v3[0], v3[0], v3[1], ALU.add))
                    for b in range(NB):
                        ins = V.max(v3[2][:, b, :], v3[0][:, b, :])
                    st.step(ins)
                    for b in range(NB):
                        ins = V.max_index(idx[:, b, :], v3[2][:, b, :], v3[0][:, b, :])
                    st.step(ins)
                    V.tensor_copy(v3[3], idx)
                    V.tensor_tensor(v1[1], v3[2][:, :, 1], v3[2][:, :, 0], ALU.subtract).then_inc(g_d, 1)
                    dve.wait_ge(g_e, 1)
                    st.step(V.tensor_scalar_add(v1[2], v1[1], 1.0))
                    st.step(V.reciprocal(v1[2], v1[2]))
                    st.step(V.tensor_tensor(v1[3], v1[1], v1[2], ALU.mult))
                    for j in range(2):
                        st.step(V.tensor_tensor(v3[j], row(iota_f[:, 0:NE]), wide(v3[3][:, :, j]), ALU.is_equal))
                        st.step(V.tensor_tensor(v3[j], v3[j], wide(v1[2 + j]), ALU.mult))
                    V.tensor_tensor(v3[0], v3[0], v3[1], ALU.add).then_inc(g_ready, 1)

        def experts():
            L = "_e"
            GX = KC * SUP
            hid = [edges[:, 2 * GX + k * SUP:2 * GX + (k + 1) * SUP] if k < 7 else
                   ring[:, (k - 7) * SUP:(k - 6) * SUP] for k in range(HK)]
            gs = ring[0:NE, 5 * SUP + HK * P:6 * SUP + HK * P]
            relu, quad, mid, res = xn, tmp, [v.rearrange("p k n -> p (k n)") for v in xT], raw
            xg_in, h_ps, relu_ready, gate_ps, gated, hid_ready, y_ps, y_ready = (
                sem(n + L) for n in ("xg_in", "h_ps", "relu", "gate_ps", "gated", "hid", "y_ps", "y_ready"))
            mid_in, res_st, stored, chain_v, h_all, gs_ready = (
                [sem(f"mid_in{j}" + L) for j in range(2)], sem("res_st" + L), sem("stored" + L), sem("dve" + L),
                sem("h_all" + L), sem("gs" + L))
            tick_a = sem("tick_a" + L)
            before = {0: 5, 1: 4}
            halves = lambda v: v[:, 0:SUP].rearrange("p (a n) -> p a n", a=2)
            with nc.Block() as block:
                @block.sync
                def _(sp):
                    def load_group(g):
                        for j in range(SB):
                            dst = edges[:, ds((g % 2) * GX, GX)].rearrange("p (k n) -> p k n", k=KC)[:, :, j * P:(j + 1) * P]
                            sp.dma_start(dst, mid_featT[ds(g * SB + j, 1), :, :].rearrange("a p (k n) -> (a p) k n", k=KC)
                                         ).then_inc(xg_in, 16)

                    def load_mid(g, j):
                        sp.wait_ge(y_ready, g * SB + before.get(j, j + 4))
                        sp.dma_start(mid[j % 2], mid_rows[ds((g * SB + j) * P, P), :]).then_inc(mid_in[j % 2], 16)

                    def store(g, j):
                        sp.wait_ge(y_ready, g * SB + (j + 6))
                        sp.dma_start(out[ds((g * SB + j) * P, P), :], res[j % 2][:, 0:C]).then_inc(res_st, 16)
                        sp.wait_ge(res_st, (g * SB + (j + 1)) * 16)
                        sp.sem_inc(stored, 1)

                    def group(g, more):
                        if more:
                            sp.wait_ge(xg_in, (g + 1) * (16 * SB))
                            sp.wait_ge(h_all, g + 1)
                            load_group(g + 1)
                        load_mid(g, 0)
                        for j in range(SB):
                            if j + 1 < SB:
                                load_mid(g, j + 1)
                            store(g, j)
                    sp.sem_inc(stored, 5)
                    load_group(0)
                    with sp.Fori(0, NS - 1) as g:
                        group(g, True)
                    group(NS - 1, False)

                @block.tensor
                def _(pe):
                    pe.sem_inc(h_all, 1)
                    pe.sem_inc(y_ps, 1)
                    with pe.Fori(0, NS) as g:
                        pe.wait_ge(xg_in, (g + 1) * (16 * SB))
                        for k in range(HK):
                            pe.wait_ge(relu_ready, g * HK + (k + 1))
                            for half in range(2):
                                for c in range(KC):
                                    m = nc.tensor.matmul(acc[:, 2 * (k % 2) + half, 0:SH], w1e[:, c, k * P:(k + 1) * P],
                                                         edges[:, ds((g % 2) * GX + (c * SUP + half * SH), SH)],
                                                         start=(c == 0), stop=(c == KC - 1))
                            m.then_inc(h_ps, 1)
                            if k == 0:
                                pe.wait_ge(gs_ready, g + 1)
                                pe.wait_ge(y_ready, g * SB + 4)
                            pe.wait_ge(gated, g * HK + (k + 1))
                            for half in range(2):
                                m = nc.tensor.matmul(tps[:, half, 0:SH], pick[:, k, :], gs[:, half * SH:(half + 1) * SH],
                                                     start=True, stop=True)
                            m.then_inc(gate_ps, 1)
                        pe.sem_inc(h_all, 1)
                        pe.wait_ge(hid_ready, g * HK + (HK + 2))
                        for j in range(SB):
                            bank = tps if j % 2 else mps
                            pe.wait_ge(y_ready, g * SB + before.get(j, j + 4))
                            for k in range(HK):
                                for c in range(2):
                                    nc.tensor.matmul(bank[:, c, 0:C // 2], hid[k][:, j * P:(j + 1) * P],
                                                     w2e[:, k, c * (C // 2):(c + 1) * (C // 2)], start=(k == 0), stop=False)
                            for c in range(2):
                                m = nc.tensor.matmul(bank[:, c, 0:C // 2], gs[:, j * P:(j + 1) * P],
                                                     b2_rows[:, c * (C // 2):(c + 1) * (C // 2)], start=False, stop=True)
                            m.then_inc(y_ps, 1)

                @block.scalar
                def _(act):
                    act.sem_inc(relu_ready, 2)
                    with act.Fori(0, NS) as g:
                        act.wait_ge(y_ps, g * SB + 1)
                        act.sem_inc(tick_a, 1)
                        nc.scalar.activation(gs, gatesT[:, ds(g * SUP, SUP)], ACT.Copy).then_inc(gs_ready, 1)
                        for k in range(HK):
                            act.wait_ge(h_ps, g * HK + (k + 1))
                            act.wait_ge(hid_ready, g * HK + (k + 1))
                            nc.scalar.activation(halves(relu[k % 2]), acc[:, 2 * (k % 2):2 * (k % 2) + 2, 0:SH], ACT.Relu,
                                                 bias=b1col[:, k:k + 1]).then_inc(relu_ready, 1)

                @block.vector
                def _(dve):
                    st = Steps(dve, chain_v)
                    V = nc.vector
                    dve.sem_inc(gated, 1)
                    dve.sem_inc(hid_ready, 2)
                    dve.sem_inc(y_ready, 5)
                    with dve.Fori(0, NS) as g:
                        st.loop(g, HK)
                        for k in range(HK):
                            dve.wait_ge(relu_ready, g * HK + (k + 3))
                            dve.wait_ge(gate_ps, g * HK + (k + 1))
                            dve.wait_ge(y_ps, g * SB + 1)
                            st.step(V.tensor_tensor(halves(quad[k % 2]), halves(relu[k % 2]), tps[:, :, 0:SH], ALU.mult))
                            dve.sem_inc(gated, 1)
                            V.tensor_tensor(hid[k], quad[k % 2][:, 0:SUP], relu[k % 2][:, 0:SUP], ALU.mult).then_inc(hid_ready, 1)
                        for j in range(SB):
                            dve.wait_ge(y_ps, g * SB + (j + 2))
                            dve.wait_ge(mid_in[j % 2], (g * (2 if j % 2 else 3) + (j // 2 + 1)) * 16)
                            dve.wait_ge(stored, g * SB + before.get(j, j + 4))
                            V.tensor_tensor(res[j % 2][:, 0:C].rearrange("p (a n) -> p a n", a=2), (tps if j % 2 else mps)[:, :, 0:C // 2],
                                            mid[j % 2].rearrange("p (a n) -> p a n", a=2), ALU.add).then_inc(y_ready, 1)
                    st.done(NS)

        run(setup)
        if upto >= 1:
            run(features, 0)
        if upto >= 2:
            run(transform, 0)
        if upto >= 3:
            run(scores, 0)
        if upto >= 4:
            run(aggregate, 0)
        if upto >= 5:
            run(features, 1)
        if upto >= 6:
            run(transform, 1)
        if upto >= 7:
            run(scores, 1)
        if upto >= 8:
            run(aggregate, 1)
        if upto >= 9:
            run(route)
        if upto >= 10:
            run(experts)


INPUTS = dict(x="x", W0="L0_gnn_W1", a_src0="L0_gnn_a_src1", a_dst0="L0_gnn_a_dst1", b1g="L0_gnn_b1",
              W1="L0_gnn_W2", a_src1="L0_gnn_a_src2", a_dst1="L0_gnn_a_dst2", b2g="L0_gnn_b2", emb="L0_ffn_router_emb", probe_w="L0_ffn_probe_w", fatigue="L0_ffn_fatigue",
              energy="L0_ffn_energy", b2_rows="L0_ffn_b2")
DEBUG = ()
UPTO = 99


def kernel(**inputs):
    import numpy as np
    import concourse.bacc as bacc
    from concourse.bass_utils import run_bass_kernel_spmd

    src, dst = np.asarray(inputs["src"]), np.asarray(inputs["dst"])
    src = np.concatenate([src, np.zeros(EP - E, src.dtype)])
    dst = np.concatenate([dst, np.full(EP - E, NP - 1, dst.dtype)])
    arrays = {k: np.ascontiguousarray(inputs[v]) for k, v in INPUTS.items()}
    arrays["x"] = np.concatenate([arrays["x"], np.zeros((NP - N, C), np.float32)])
    for l in range(2):
        for n in ("a_src", "a_dst"):
            arrays[f"{n}{l}"] = arrays[f"{n}{l}"].reshape(C)
    arrays["src_p"] = src.reshape(P, NT)
    arrays["src_t"] = np.ascontiguousarray(src.reshape(NT, P).T)
    arrays["dst_t"] = np.ascontiguousarray(dst.reshape(NT, P).T)
    arrays["dst_halo"] = np.concatenate([dst[:1] * 0 - 1, dst, dst[:1] * 0 + NP])
    arrays["dst_last"] = np.concatenate([dst[:1] * 0, dst.reshape(NT, P)[:, -1]]).reshape(1, NT + 1)
    for name, part in (("w_fast", "w_fast"), ("w_slow", "w_slow"), ("w_hebb", "h_fast")):
        up = np.asarray(inputs[f"L0_ffn_{part}1"]).transpose(1, 0, 2).reshape(KC, P, 2, C).transpose(0, 2, 1, 3)
        down = np.asarray(inputs[f"L0_ffn_{part}2"]).reshape(HK, P, C)
        arrays[name] = np.concatenate([up.reshape(2 * KC, P, C), down])
    g1 = np.broadcast_to(np.asarray(inputs["L0_ffn_m_gate1"]).reshape(1, 1, 2, 4), (P, KC, 2, 4)).reshape(P, 2 * KC, 4)
    g2 = np.broadcast_to(np.asarray(inputs["L0_ffn_m_gate2"])[:, None], (NE, HID)).reshape(HK, P).T
    arrays["w_scale"] = np.concatenate([g1, np.broadcast_to(g2[:, :, None], (P, HK, 4))], 1).reshape(P, 4 * UNITS)
    arrays["route_wT"] = np.concatenate([np.asarray(inputs["L0_ffn_router_w"]), arrays["probe_w"]]).T.copy()
    arrays["b1_col"] = np.asarray(inputs["L0_ffn_b1"]).reshape(HK, P).T.copy()
    arrays = {k: np.ascontiguousarray(a) for k, a in arrays.items()}
    nc = bacc.Bacc("TRN2", target_bir_lowering=False, num_devices=1)
    io = {k: nc.dram_tensor("in_" + k, a.shape, mybir.dt.from_np(a.dtype), kind="ExternalInput").ap()
          for k, a in arrays.items()}
    io["bend"] = io["dst_last"]
    shapes = {"score_tab0": (NP, 8), "score_tab1": (NP, 1), "first_val0": (EP, 8), "first_val1": (EP, 1), "edge_ex0": (EP, 8),
              "edge_ex1": (EP, 1), "feat_tab0": (NP, ROW), "feat_tab1": (NP, ROW), "agg_raw0": (NP, ROW), "agg_raw1": (NP, ROW)}
    dbg = {n: nc.dram_tensor("dbg_" + n, shapes[n], f32, kind="ExternalOutput").ap() for n in DEBUG}
    outp = nc.dram_tensor("out_rows", (NP, C), f32, kind="ExternalOutput").ap() if not DEBUG else None
    gnn_ffn(nc, io, outp, UPTO, dbg)
    r = run_bass_kernel_spmd(nc, [{"in_" + k: a for k, a in arrays.items()}], core_ids=[0])
    if DEBUG:
        return tuple(r.results[0]["dbg_" + n] for n in DEBUG)
    return r.results[0]["out_rows"][:N]
```
